# Optimizing a Trainium2 kernel written in Bass

```python
import numpy as np
import jax
import jax.numpy as jnp

def _softmax(x, axis=-1):
    return jax.nn.softmax(x, axis=axis)

def _gelu(x):
    return jax.nn.gelu(x, approximate=True)

def _silu(x):
    return jax.nn.silu(x)

def _sigmoid(x):
    return jax.nn.sigmoid(x)

def _layernorm(x, axis=-1, eps=1e-05):
    m = jnp.mean(x, axis=axis, keepdims=True)
    v = jnp.var(x, axis=axis, keepdims=True)
    return (x - m) / jnp.sqrt(v + eps)

def _scatter_add(tgt, idx, src, axis=0):
    return tgt.at[idx].add(src)

def _segment_sum(src, seg, n):
    return jax.ops.segment_sum(src, seg, n)
kernel_name = 'mk_gnn_preln_d4_gnn_r32_4867d9'

def setup_inputs(seed: int=0):
    np.random.seed(seed)
    _w = jnp.asarray

    def _rec_inputs():
        import jax
        import jax.numpy as jnp
        _gk = jax.random.key(seed)
        x = -0.0003713 + 1 * jax.random.normal(jax.random.fold_in(_gk, 1), (50000, 128), jnp.float32)
        src = jax.random.randint(jax.random.fold_in(_gk, 2), (50000,), 0, 50000, jnp.int32)
        dst = jax.random.randint(jax.random.fold_in(_gk, 3), (50000,), 0, 50000, jnp.int32)
        _o = jnp.argsort(dst, stable=True)
        src = src[_o]
        dst = dst[_o]
        edge_type_4 = jax.random.randint(jax.random.fold_in(_gk, 14), (50000,), 0, 4, jnp.int32)
        edge_weight = jax.random.uniform(jax.random.fold_in(_gk, 15), (50000,), jnp.float32, 0.0, 0.999996)
        edge_weight_n2 = jax.random.uniform(jax.random.fold_in(_gk, 16), (50000,), jnp.float32, 0.0, 0.999996)
        return (x, src, dst, edge_type_4, edge_weight, edge_weight_n2)
    x, src, dst, edge_type_4, edge_weight, edge_weight_n2 = _rec_inputs()

    def _L0_gnn_setup():
        import jax, jax.numpy as jnp
        import numpy as np
        N_NODES = 3125
        N_EDGES = 100000
        D_IN = 128
        D_OUT = 128
        key = jax.random.key(seed)
        k1, k2, k3, k4 = jax.random.split(key, 4)
        x = jax.random.normal(k1, (N_NODES, D_IN), dtype=jnp.float32)
        edge_index = jax.random.randint(k2, (2, N_EDGES), 0, N_NODES, dtype=jnp.int64)
        W = jax.random.normal(k3, (D_IN, D_OUT), dtype=jnp.float32) * (1.0 / np.sqrt(D_IN))
        b = jax.random.normal(k4, (D_OUT,), dtype=jnp.float32) * 0.01
        batch = jnp.zeros((N_NODES,), dtype=jnp.int64)
        return {'x': x, 'edge_index': edge_index, 'batch': batch, 'W': W, 'b': b}
    _L0_gnn_all = _L0_gnn_setup()
    _L0_gnn_in = {k: v for k, v in _L0_gnn_all.items() if k in ('W', 'b')}
    del _L0_gnn_all

    def _L1_gnn_setup():
        import jax, jax.numpy as jnp
        import numpy as np
        NUM_RELATIONS = 4
        N_NODES = 625
        N_EDGES = 10000
        F_IN = 128
        HID = 128
        EMB = 128

        def _rgcn_conv(x, src, dst, edge_type, edge_weight, W, root, bias):
            xj = x[src]
            m = jnp.zeros((xj.shape[0], W.shape[2]), dtype=x.dtype)
            for r in range(W.shape[0]):
                mask = (edge_type == r).astype(x.dtype)[:, None]
                m = m + mask * (xj @ W[r])
            m = m * edge_weight[:, None]
            out = jax.ops.segment_sum(m, dst, num_segments=x.shape[0])
            return out + x @ root + bias
        key = jax.random.key(seed)
        ks = jax.random.split(key, 10)
        return {'x': jax.random.normal(ks[0], (N_NODES, F_IN), dtype=jnp.float32), 'edge_index': jax.random.randint(ks[1], (2, N_EDGES), 0, N_NODES, dtype=jnp.int64 if jax.config.jax_enable_x64 else jnp.int32).astype(jnp.int32), 'edge_type': jax.random.randint(ks[2], (N_EDGES,), 0, NUM_RELATIONS).astype(jnp.int32), 'edge_weight': jax.random.uniform(ks[3], (N_EDGES,), dtype=jnp.float32), 'W1': jax.random.normal(ks[4], (NUM_RELATIONS, F_IN, HID), dtype=jnp.float32) * 0.05, 'root1': jax.random.normal(ks[5], (F_IN, HID), dtype=jnp.float32) * 0.05, 'b1': jax.random.normal(ks[6], (HID,), dtype=jnp.float32) * 0.05, 'W2': jax.random.normal(ks[7], (NUM_RELATIONS, HID, EMB), dtype=jnp.float32) * 0.05, 'root2': jax.random.normal(ks[8], (HID, EMB), dtype=jnp.float32) * 0.05, 'b2': jax.random.normal(ks[9], (EMB,), dtype=jnp.float32) * 0.05}
    _L1_gnn_all = _L1_gnn_setup()
    _L1_gnn_in = {k: v for k, v in _L1_gnn_all.items() if k in ('W1', 'root1', 'b1', 'W2', 'root2', 'b2')}
    del _L1_gnn_all

    def _L2_gnn_setup():
        import jax, jax.numpy as jnp
        import numpy as np
        N_NODES = 3125
        N_EDGES = 50000
        D = 128
        BN_EPS = 1e-05
        key = jax.random.key(seed)
        ks = jax.random.split(key, 10)
        s = 1.0 / np.sqrt(D)
        s2 = 1.0 / np.sqrt(2 * D)
        return {'feat': jax.random.normal(ks[0], (N_NODES, D), dtype=jnp.float32), 'src': jax.random.randint(ks[1], (N_EDGES,), 0, N_NODES, dtype=jnp.int32), 'dst': jax.random.randint(ks[2], (N_EDGES,), 0, N_NODES, dtype=jnp.int32), 'iw': jax.random.uniform(ks[3], (N_EDGES,), dtype=jnp.float32), 'ow': jax.random.uniform(ks[4], (N_EDGES,), dtype=jnp.float32), 'bn_gamma': jnp.ones((D,), jnp.float32), 'bn_beta': jnp.zeros((D,), jnp.float32), 'W_in': jax.random.normal(ks[5], (D, D), jnp.float32) * s, 'b_in': jnp.zeros((D,), jnp.float32), 'W_out': jax.random.normal(ks[6], (D, D), jnp.float32) * s, 'b_out': jnp.zeros((D,), jnp.float32), 'Wg_in': jax.random.normal(ks[7], (2 * D, 2 * D), jnp.float32) * s2, 'bg_in': jnp.zeros((2 * D,), jnp.float32), 'Wg_out': jax.random.normal(ks[8], (D, 2 * D), jnp.float32) * s}
    _L2_gnn_all = _L2_gnn_setup()
    _L2_gnn_in = {k: v for k, v in _L2_gnn_all.items() if k in ('bn_gamma', 'bn_beta', 'W_in', 'b_in', 'W_out', 'b_out', 'Wg_in', 'bg_in', 'Wg_out')}
    del _L2_gnn_all

    def _L3_gnn_setup():
        import jax, jax.numpy as jnp
        import numpy as np
        N = 50000
        E = 18750
        D = 128
        L = 3
        key = jax.random.key(seed)
        ks = jax.random.split(key, 2 + 2 * L)
        x = jax.random.normal(ks[0], (N, D), dtype=jnp.float32)
        edge_index = jax.random.randint(ks[1], (2, E), 0, N, dtype=jnp.int32)
        s = float(np.sqrt(6.0 / (D + D)))
        inp = {'x': x, 'edge_index': edge_index}
        for i in range(L):
            inp[f'W{i}'] = jax.random.uniform(ks[2 + 2 * i], (D, D), jnp.float32, -s, s)
            inp[f'b{i}'] = jax.random.uniform(ks[3 + 2 * i], (D,), jnp.float32, -0.01, 0.01)
        return inp
    _L3_gnn_all = _L3_gnn_setup()
    _L3_gnn_in = {k: v for k, v in _L3_gnn_all.items() if k in ('W0', 'b0', 'W1', 'b1', 'W2', 'b2')}
    del _L3_gnn_all
    return {'x': x, 'src': src, 'dst': dst, 'edge_type_4': edge_type_4, 'edge_weight': edge_weight, 'edge_weight_n2': edge_weight_n2, 'L0_gnn_W': _L0_gnn_in['W'], 'L0_gnn_b': _L0_gnn_in['b'], 'L1_gnn_W1': _L1_gnn_in['W1'], 'L1_gnn_root1': _L1_gnn_in['root1'], 'L1_gnn_b1': _L1_gnn_in['b1'], 'L1_gnn_W2': _L1_gnn_in['W2'], 'L1_gnn_root2': _L1_gnn_in['root2'], 'L1_gnn_b2': _L1_gnn_in['b2'], 'L2_gnn_bn_gamma': _L2_gnn_in['bn_gamma'], 'L2_gnn_bn_beta': _L2_gnn_in['bn_beta'], 'L2_gnn_W_in': _L2_gnn_in['W_in'], 'L2_gnn_b_in': _L2_gnn_in['b_in'], 'L2_gnn_W_out': _L2_gnn_in['W_out'], 'L2_gnn_b_out': _L2_gnn_in['b_out'], 'L2_gnn_Wg_in': _L2_gnn_in['Wg_in'], 'L2_gnn_bg_in': _L2_gnn_in['bg_in'], 'L2_gnn_Wg_out': _L2_gnn_in['Wg_out'], 'L3_gnn_W0': _L3_gnn_in['W0'], 'L3_gnn_b0': _L3_gnn_in['b0'], 'L3_gnn_W1': _L3_gnn_in['W1'], 'L3_gnn_b1': _L3_gnn_in['b1'], 'L3_gnn_W2': _L3_gnn_in['W2'], 'L3_gnn_b2': _L3_gnn_in['b2']}

def reference(x, src, dst, edge_type_4, edge_weight, edge_weight_n2, L0_gnn_W, L0_gnn_b, L1_gnn_W1, L1_gnn_root1, L1_gnn_b1, L1_gnn_W2, L1_gnn_root2, L1_gnn_b2, L2_gnn_bn_gamma, L2_gnn_bn_beta, L2_gnn_W_in, L2_gnn_b_in, L2_gnn_W_out, L2_gnn_b_out, L2_gnn_Wg_in, L2_gnn_bg_in, L2_gnn_Wg_out, L3_gnn_W0, L3_gnn_b0, L3_gnn_W1, L3_gnn_b1, L3_gnn_W2, L3_gnn_b2):
    import jax
    import jax.numpy as jnp

    def _L0_gnn_ref(x, edge_index, batch, W, b):
        import jax, jax.numpy as jnp
        import numpy as np
        N_NODES = 3125
        N_EDGES = 100000
        D_IN = 128
        D_OUT = 128
        N = x.shape[0]
        xw = x @ W
        loop = jnp.arange(N, dtype=edge_index.dtype)
        row = jnp.concatenate([edge_index[0], loop])
        col = jnp.concatenate([edge_index[1], loop])
        deg = jax.ops.segment_sum(jnp.ones_like(col, dtype=xw.dtype), col, num_segments=N)
        dinv = jnp.where(deg > 0, jax.lax.rsqrt(deg), 0.0)
        norm = dinv[row] * dinv[col]
        msg = xw[row] * norm[:, None]
        out = jax.ops.segment_sum(msg, col, num_segments=N) + b
        return out

    def _L1_gnn_ref(x, edge_index, edge_type, edge_weight, W1, root1, b1, W2, root2, b2):
        import jax, jax.numpy as jnp
        import numpy as np
        NUM_RELATIONS = 4
        N_NODES = 625
        N_EDGES = 10000
        F_IN = 128
        HID = 128
        EMB = 128

        def _rgcn_conv(x, src, dst, edge_type, edge_weight, W, root, bias):
            xj = x[src]
            m = jnp.zeros((xj.shape[0], W.shape[2]), dtype=x.dtype)
            for r in range(W.shape[0]):
                mask = (edge_type == r).astype(x.dtype)[:, None]
                m = m + mask * (xj @ W[r])
            m = m * edge_weight[:, None]
            out = jax.ops.segment_sum(m, dst, num_segments=x.shape[0])
            return out + x @ root + bias
        src, dst = (edge_index[0], edge_index[1])
        ew = (edge_weight - edge_weight.min()) / (edge_weight.max() - edge_weight.min() + 1e-08)
        h = jax.nn.relu(_rgcn_conv(x, src, dst, edge_type, ew, W1, root1, b1))
        h = _rgcn_conv(h, src, dst, edge_type, ew, W2, root2, b2)
        return h

    def _L2_gnn_ref(feat, src, dst, iw, ow, bn_gamma, bn_beta, W_in, b_in, W_out, b_out, Wg_in, bg_in, Wg_out):
        import jax, jax.numpy as jnp
        import numpy as np
        N_NODES = 3125
        N_EDGES = 50000
        D = 128
        BN_EPS = 1e-05
        n = feat.shape[0]
        mu = jnp.mean(feat, axis=0)
        var = jnp.var(feat, axis=0)
        x = (feat - mu) * jax.lax.rsqrt(var + BN_EPS) * bn_gamma + bn_beta
        feat_in = x @ W_in + b_in
        feat_out = x @ W_out + b_out
        a_in = jax.ops.segment_sum(feat_in[src] * iw[:, None], dst, num_segments=n)
        a_out = jax.ops.segment_sum(feat_out[dst] * ow[:, None], src, num_segments=n)
        a = jnp.concatenate((a_in, a_out), axis=1)
        f = a @ Wg_in + bg_in
        f_i, f_n = jnp.split(f, 2, axis=1)
        b = x @ Wg_out
        b_z, b_h = jnp.split(b, 2, axis=1)
        input_gate = jax.nn.sigmoid(f_i + b_z)
        new_gate = jnp.tanh(f_n + b_h)
        return new_gate + input_gate * (x - new_gate)

    def _L3_gnn_ref(x, edge_index, W0, b0, W1, b1, W2, b2):
        import jax, jax.numpy as jnp
        import numpy as np
        N = 50000
        E = 18750
        D = 128
        L = 3
        n = x.shape[0]
        loops = jnp.arange(n, dtype=edge_index.dtype)
        src = jnp.concatenate([edge_index[0], loops])
        dst = jnp.concatenate([edge_index[1], loops])
        deg = jax.ops.segment_sum(jnp.ones(src.shape, jnp.float32), dst, num_segments=n)
        dis = jnp.where(deg > 0, jax.lax.rsqrt(deg), 0.0)
        norm = dis[src] * dis[dst]

        def gcn_layer(h, W, b):
            h = h @ W
            msg = h[src] * norm[:, None]
            out = jax.ops.segment_sum(msg, dst, num_segments=n)
            return out + b
        h = gcn_layer(x, W0, b0)
        h = jax.nn.relu(h)
        h = gcn_layer(h, W1, b1)
        h = jax.nn.relu(h)
        h = gcn_layer(h, W2, b2)
        return h
    edge_index = jnp.stack([src, dst])
    batch0 = jnp.zeros((50000,), jnp.int32)
    h = jnp.maximum(_layernorm(x, axis=-1), 0.0)
    x = x + _L0_gnn_ref(h, edge_index, batch0, L0_gnn_W, L0_gnn_b)
    h = jnp.maximum(_layernorm(x, axis=-1), 0.0)
    x = x + _L1_gnn_ref(h, edge_index, edge_type_4, edge_weight, L1_gnn_W1, L1_gnn_root1, L1_gnn_b1, L1_gnn_W2, L1_gnn_root2, L1_gnn_b2)
    h = jnp.maximum(_layernorm(x, axis=-1), 0.0)
    x = x + _L2_gnn_ref(h, src, dst, edge_weight, edge_weight_n2, L2_gnn_bn_gamma, L2_gnn_bn_beta, L2_gnn_W_in, L2_gnn_b_in, L2_gnn_W_out, L2_gnn_b_out, L2_gnn_Wg_in, L2_gnn_bg_in, L2_gnn_Wg_out)
    h = jnp.maximum(_layernorm(x, axis=-1), 0.0)
    x = x + _L3_gnn_ref(h, edge_index, L3_gnn_W0, L3_gnn_b0, L3_gnn_W1, L3_gnn_b1, L3_gnn_W2, L3_gnn_b2)
    return x

_drawn_inputs = setup_inputs


def setup_inputs(seed=0):
    import zlib

    import numpy as np

    out = dict(_drawn_inputs(seed))
    spreads = {'L2_gnn_bn_gamma': (1.0, 0.2),
     'L2_gnn_bn_beta': (0.0, 0.1),
     'L2_gnn_b_in': (0.0, 0.638),
     'L2_gnn_b_out': (0.0, 0.71),
     'L2_gnn_bg_in': (0.0, 0.324)}
    factors = {'L0_gnn_b': 8.0,
     'L1_gnn_b1': 3.283,
     'L3_gnn_b0': 32.126,
     'L3_gnn_b1': 8.0,
     'L3_gnn_b2': 8.0}
    for name, (base, spread) in spreads.items():
        noise = np.random.default_rng([zlib.crc32(name.encode()), seed]).standard_normal(out[name].shape)
        drawn = base * np.exp(spread * noise) if base else spread * noise
        out[name] = jnp.asarray(drawn.astype(out[name].dtype))
    for name, factor in factors.items():
        out[name] = (out[name] * factor).astype(out[name].dtype)
    return out
```

```python
import concourse.bass as bass
from concourse import mybir
import numpy as np

F32 = mybir.dt.float32
BF16 = mybir.dt.bfloat16
I32 = mybir.dt.int32
ALU = mybir.AluOpType
ACT = mybir.ActivationFunctionType
AXX = mybir.AxisListType.X

NODES, EDGES, D, TYPES = 50000, 50000, 128, 4
P = 128
J = 4
GN = P * J
NG = -(-NODES // GN)
NPAD = NG * GN
PAIRS = NG // 2
LAST_P = (NODES - (NG - 1) * GN) // J
TILES = 5
CAP = TILES * P
ROUNDS = -(-EDGES // CAP)
EP, ET = 125, 400
MW = 8
W_NODE, W_TYPED, W_COL, W_EW, W_PLAIN = range(5)
BIG = 1 << 20
EPS = 1e-5
UN = 8
assert NG % 2 == 0 and EP * ET == EDGES and ET % (2 * UN) == 0 and LAST_P * J + (NG - 1) * GN == NODES


class Scope:

    def __init__(self, nc, prefix):
        self.nc, self.prefix = nc, prefix

    def sb(self, name, shape, dt):
        return self.nc.alloc_sbuf_tensor(f"{self.prefix}_{name}", shape, dt)

    def ps(self, name, shape, dt):
        return self.nc.alloc_psum_tensor(f"{self.prefix}_{name}", shape, dt)

    def sem(self, name):
        return self.nc.alloc_semaphore(f"{self.prefix}_{name}")


class Mem:

    def __init__(self, nc):
        def dram(name, shape, dt=F32):
            return nc.dram_tensor(name, shape, dt).ap()

        self.meta = {s: dram(f"meta_{s}", [ROUNDS * NG * CAP, MW], I32) for s in ("fwd", "rev")}
        self.X = dram("x_state", [NPAD, D])
        self.A = dram("table_a", [NPAD, D])
        self.B = dram("table_b", [NPAD, D])
        self.typed = [dram(f"typed_{i}", [NPAD, TYPES * D]) for i in range(2)]
        self.hT = [dram(f"hT_{i}", [NG * P, GN]) for i in range(2)]
        self.aggT = dram("agg_out_T", [NG * P, GN])
        self.sq = dram("sqrt_degree", [NG, GN])
        sb = nc.alloc_sbuf_tensor
        self.ident = sb("ident", [P, P], F32)
        self.iota = sb("iota", [P, GN], F32)
        self.dinv = sb("dinv", [P, NG * J], F32)
        self.dinv2 = sb("dinv2", [P, NG * J], F32)
        self.sum_out = sb("sum_out", [P, NG * J], F32)
        self.bn = sb("bn", [P, 2], F32)
        self.rounds = sb("rounds", [1, 1], I32)
        self.eps = sb("eps", [P, 1], F32)
        self.gath = [[sb(f"gath_{p}_{k}", [P, D + 1], F32) for k in range(TILES)] for p in range(2)]


def rows(ap, g, n=P):
    w = ap.shape[1]
    v = ap[bass.ds(g * GN, n * J), :] if not isinstance(g, int) else ap[g * GN:g * GN + n * J, :]
    return v.rearrange("(p j) d -> p (j d)", j=J)


def group(ap, g, n):
    return ap[g * n:(g + 1) * n, :] if isinstance(g, int) else ap[bass.ds(g * n, n), :]


def col(ap, c, n=1):
    return ap[:, c:c + n] if isinstance(c, int) else ap[:, bass.ds(c, n)]


class Link:

    def __init__(self, eng, sem, base=0):
        self.eng, self.sem, self.base, self.n = eng, sem, base, 0

    def __call__(self, ins):
        ins.then_inc(self.sem, 1)
        self.n += 1
        return self

    def wait(self):
        self.eng.wait_ge(self.sem, self.base + self.n)


def constants(nc, m):
    with nc.cleanup_on_exit():
        s_zero, s_done = nc.alloc_semaphore("c_zero"), nc.alloc_semaphore("c_done")
        with nc.Block() as block:
            @block.gpsimd
            def _(pool):
                pool.memset(m.ident[:, :], 0.0).then_inc(s_zero, 1)
                pool.iota(m.iota[:, :], [[1, GN]], base=0, channel_multiplier=0,
                          allow_small_or_imprecise_dtypes=True).then_inc(s_done, 1)
                pool.wait_ge(s_zero, 1)
                pool.affine_select(out=m.ident[:, :], in_=m.ident[:, :], compare_op=ALU.not_equal, fill=1.0,
                                   base=0, pattern=[[-1, P]], channel_multiplier=1).then_inc(s_done, 1)

            @block.vector
            def _(dve):
                for p in range(2):
                    for k in range(TILES):
                        dve.memset(m.gath[p][k][:, :], 1.0)
                dve.memset(m.eps[:, :], EPS).then_inc(s_done, 1)
                dve.wait_ge(s_done, 3)


def place_edges(nc, m, src, dst, etype, w_in, w_out):
    with nc.cleanup_on_exit():
        sb, sem = nc.alloc_sbuf_tensor, nc.alloc_semaphore
        ps = nc.alloc_psum_tensor
        ends = {"fwd": sb("dst_sb", [EP, ET], I32), "rev": sb("src_sb", [EP, ET], I32)}
        et = sb("type_sb", [EP, ET], I32)
        ws = {"fwd": sb("w_in_sb", [EP, ET], F32), "rev": sb("w_out_sb", [EP, ET], F32)}
        ew = sb("ew_sb", [EP, ET], F32)
        ti, tj = sb("tmp_i", [EP, ET], I32), sb("tmp_j", [EP, ET], I32)
        typed = sb("typed_sb", [EP, ET], I32)
        grp = {s: sb(f"grp_{s}", [EP, ET], F32) for s in ends}
        cols = {s: sb(f"cols_{s}", [EP, ET], F32) for s in ends}
        rank = {s: sb(f"rank_{s}", [EP, ET], F32) for s in ends}
        before = sb("before", [EP, EP], BF16)
        after = sb("after", [EP, EP], BF16)
        zeros = sb("zeros", [1, GN], BF16)
        ones = sb("ones", [1, P], F32)
        wm, wr, wb = sb("w_mm", [EP, 2], F32), sb("w_mr", [1, 2], F32), sb("w_mb", [EP, 4], F32)
        RING = 4
        hot = {s: [sb(f"hot_{s}{i}", [EP, NG], BF16) for i in range(RING)] for s in ends}
        hotc = [sb(f"hotc{i}", [EP, GN], BF16) for i in range(RING)]
        junk = sb("junk", [EP, NG], F32)
        chunk = {s: sb(f"rank8_{s}", [EP, UN], F32) for s in ends}
        cnt = sb("cnt", [EP, 2], F32)
        steps = sb("steps", [1, ROUNDS], F32)
        stepj, rf = sb("step_junk", [1, ROUNDS], F32), sb("rounds_f", [1, 1], F32)
        deg, sqd = sb("deg", [NG, GN], F32), sb("sqd", [NG, GN], F32)
        rdeg = sb("rdeg", [P, J * NG], F32)
        pr = {s: ps(f"p_{s}", [EP, 512], F32) for s in ends}
        ph = ps("p_hist", [NG, GN], F32)
        pt = ps("p_t", [P, 512], F32)

        s_load, s_c, s_dve, s_zero = sem("e_load"), sem("e_const"), sem("e_dve"), sem("e_zero")
        s_hot, s_rank, s_ranked, s_rest = sem("e_hot"), sem("e_rank"), sem("e_ranked"), sem("e_rest")
        s_mt, s_mr, s_mb, s_sq, s_dt, s_st = (sem(n) for n in ("e_mt", "e_mr", "e_mb", "e_sq", "e_dt", "e_st"))
        s_deg, s_rdeg, s_copy = sem("e_deg"), sem("e_rdeg"), sem("e_copy")

        with nc.Block() as block:
            @block.sync
            def _(sp):
                for t, a in ((ends["fwd"], dst), (ends["rev"], src), (et, etype), (ws["fwd"], w_in), (ws["rev"], w_out)):
                    sp.dma_start(t[:, :], a.rearrange("(p t) -> p t", t=ET)).then_inc(s_load, 16)
                sp.wait_ge(s_sq, 1)
                sp.dma_start(m.sq[:, :], sqd[:, :]).then_inc(s_st, 16)
                sp.wait_ge(s_st, 16)

            @block.gpsimd
            def _(pool):
                pool.memset(before[:, :], 1.0).then_inc(s_zero, 1)
                pool.memset(after[:, :], 1.0).then_inc(s_zero, 1)
                pool.iota(steps[:, :], [[CAP, ROUNDS]], base=0, channel_multiplier=0,
                          allow_small_or_imprecise_dtypes=True).then_inc(s_c, 1)
                pool.wait_ge(s_zero, 2)
                pool.affine_select(out=before[:, :], in_=before[:, :], compare_op=ALU.is_gt, fill=0.0,
                                   base=0, pattern=[[1, EP]], channel_multiplier=-1).then_inc(s_c, 1)
                pool.affine_select(out=after[:, :], in_=after[:, :], compare_op=ALU.is_ge, fill=0.0,
                                   base=0, pattern=[[-1, EP]], channel_multiplier=1).then_inc(s_c, 1)

            @block.vector
            def _(dve):
                link = Link(dve, s_dve)
                link(dve.memset(zeros[:, :], 0.0))
                link(dve.memset(ones[:, :], 1.0))
                dve.wait_ge(s_load, 16 * 5)
                link.wait()
                for s in ends:
                    link(dve.tensor_scalar(ti[:, :], ends[s][:, :], 9, None, ALU.logical_shift_right)).wait()
                    link(dve.tensor_copy(grp[s][:, :], ti[:, :])).wait()
                    link(dve.tensor_scalar(ti[:, :], ends[s][:, :], 3, 7, ALU.bitwise_and, ALU.logical_shift_left))
                    link(dve.tensor_scalar(tj[:, :], ends[s][:, :], 2, 127, ALU.logical_shift_right, ALU.bitwise_and)).wait()
                    link(dve.tensor_tensor(ti[:, :], ti[:, :], tj[:, :], ALU.bitwise_or)).wait()
                    link(dve.tensor_copy(cols[s][:, :], ti[:, :])).wait()
                link(dve.tensor_scalar(ti[:, :], ends["rev"][:, :], 2, None, ALU.logical_shift_left)).wait()
                link(dve.tensor_tensor(typed[:, :], ti[:, :], et[:, :], ALU.bitwise_or))
                link(dve.reduce_max(wm[:, 0:1], ws["fwd"][:, :], AXX))
                link(dve.tensor_scalar(ew[:, :], ws["fwd"][:, :], -1.0, None, ALU.mult)).wait()
                dve.reduce_max(wm[:, 1:2], ew[:, :], AXX).then_inc(s_mt, 1)
                dve.wait_ge(s_mr, 1)
                link(dve.reduce_max(wr[:, 0:1], pt[0:1, 0:EP], AXX))
                link(dve.reduce_max(wr[:, 1:2], pt[0:1, P:P + EP], AXX)).wait()
                dve.tensor_copy(stepj[:, 0:2], wr[:, :]).then_inc(s_mt, 1)
                dve.wait_ge(s_mb, 1)
                link(dve.tensor_copy(wb[:, 0:2], pt[0:EP, 256:258])).wait()
                link(dve.tensor_scalar(wb[:, 2:3], wb[:, 0:1], wb[:, 1:2], 1e-8, ALU.add, ALU.add)).wait()
                link(dve.reciprocal(wb[:, 3:4], wb[:, 2:3])).wait()
                link(dve.tensor_scalar(ew[:, :], ws["fwd"][:, :], wb[:, 1:2], wb[:, 3:4], ALU.add, ALU.mult)).wait()
                dve.wait_ge(s_c, 3)
                dve.sem_inc(s_copy, 1)

                with dve.Fori(0, ET // UN) as i:
                    def hots(u):
                        dve.wait_ge(s_rest, i * UN + max(u + 1 - RING, 0) + 1)
                        b = u % RING
                        for s in ends:
                            dve.tensor_scalar(hot[s][b][:, :], m.iota[0:EP, 0:NG], col(grp[s], i * UN + u), None, ALU.is_equal)
                        dve.tensor_scalar(hotc[b][:, :], m.iota[0:EP, :], col(cols["fwd"], i * UN + u), None,
                                          ALU.is_equal).then_inc(s_hot, 1)

                    hots(0)
                    for u in range(UN):
                        if u + 1 < UN:
                            hots(u + 1)
                        dve.wait_ge(s_rank, i * UN + u + 1)
                        if u == 0:
                            dve.wait_ge(s_copy, 2 * i + 1)
                        for n, s in enumerate(ends):
                            if u or n:
                                dve.wait_ge(s_ranked, 2 * UN * i + 2 * u + n)
                            dve.tensor_tensor_reduce(out=junk[:, :], in0=pr[s][:, 0:NG], in1=hot[s][u % RING][:, :],
                                                     scale=1.0, scalar=0.0, op0=ALU.mult, op1=ALU.add,
                                                     accum_out=chunk[s][:, u:u + 1]).then_inc(s_ranked, 1)
                    dve.wait_ge(s_ranked, 2 * UN * i + 2 * UN)
                    for s in ends:
                        dve.tensor_copy(col(rank[s], i * UN, UN), chunk[s][:, :]).then_inc(s_copy, 1)

                dve.wait_ge(s_rest, ET + 1)
                link(dve.reduce_max(cnt[:, 0:1], pr["fwd"][:, 0:NG], AXX))
                link(dve.reduce_max(cnt[:, 1:2], pr["rev"][:, 0:NG], AXX)).wait()
                link(dve.tensor_tensor(cnt[:, 0:1], cnt[:, 0:1], cnt[:, 1:2], ALU.max)).wait()
                link(dve.tensor_scalar(stepj[:, :], steps[:, :], cnt[0:1, 0:1], 0.0, ALU.is_lt, ALU.add,
                                       accum_out=rf[:, :])).wait()
                link(dve.tensor_copy(m.rounds[:, :], rf[:, :]))
                dve.tensor_scalar(deg[:, :], ph[:, :], 1.0, None, ALU.add).then_inc(s_deg, 1)
                dve.wait_ge(s_dt, 1)
                v = m.dinv2[:, :].rearrange("p (g j) -> p j g", j=J)
                dve.reciprocal(v, pt[:, 0:J * NG].rearrange("p (j g) -> p j g", j=J)).then_inc(s_rdeg, 1)
                link.wait()
                dve.wait_ge(s_rdeg, 2)
                dve.wait_ge(s_copy, 2 * (ET // UN) + 1)

            @block.scalar
            def _(act):
                act.wait_ge(s_deg, 1)
                act.activation(sqd[:, :], deg[:, :], ACT.Sqrt).then_inc(s_sq, 1)
                act.wait_ge(s_rdeg, 1)
                act.activation(m.dinv[:, :], m.dinv2[:, :], ACT.Sqrt).then_inc(s_rdeg, 1)

            @block.tensor
            def _(pe):
                pe.wait_ge(s_mt, 1)
                pe.matmul(pt[0:1, 0:EP], wm[:, 0:1], m.ident[0:EP, 0:EP], start=True, stop=True)
                pe.matmul(pt[0:1, P:P + EP], wm[:, 1:2], m.ident[0:EP, 0:EP], start=True, stop=True).then_inc(s_mr, 1)
                pe.wait_ge(s_mt, 2)
                pe.matmul(pt[0:EP, 256:258], ones[0:1, 0:EP], stepj[0:1, 0:2], start=True, stop=True).then_inc(s_mb, 1)
                pe.wait_ge(s_dve, 2)
                for t in (pr["fwd"][:, 0:NG], pr["rev"][:, 0:NG], ph[:, :]):
                    pe.matmul(t, zeros[:, 0:t.shape[0]], zeros[:, 0:t.shape[1]], start=True, stop=True,
                              skip_group_check=True)
                pe.wait_ge(s_c, 3)
                pe.sem_inc(s_rest, 1)
                with pe.Fori(0, ET // UN) as i:
                    for u in range(UN):
                        b = u % RING
                        pe.wait_ge(s_hot, i * UN + u + 1)
                        for s in ends:
                            last = pe.matmul(pr[s][:, 0:NG], before[:, :], hot[s][b][:, :], start=False, stop=True,
                                             skip_group_check=True)
                        last.then_inc(s_rank, 1)
                        pe.matmul(ph[:, :], hot["fwd"][b][:, :], hotc[b][:, :], start=False, stop=True,
                                  skip_group_check=True)
                        pe.wait_ge(s_ranked, 2 * UN * i + 2 * u + 2)
                        for s in ends:
                            last = pe.matmul(pr[s][:, 0:NG], after[:, :], hot[s][b][:, :], start=False, stop=True,
                                             skip_group_check=True)
                        last.then_inc(s_rest, 1)
                pe.wait_ge(s_deg, 1)
                for j in range(J):
                    last = pe.matmul(pt[:, j * NG:(j + 1) * NG], deg[:, j * P:(j + 1) * P], m.ident[0:NG, 0:NG],
                                     start=True, stop=True)
                last.then_inc(s_dt, 1)

        scatter_edges(nc, m, ends, typed, grp, cols, rank, ew, ws)


def scatter_edges(nc, m, ends, typed, grp, cols, rank, ew, ws):
    sb, sem = nc.alloc_sbuf_tensor, nc.alloc_semaphore
    other = {"fwd": ends["rev"], "rev": ends["fwd"]}
    empty = sb("empty", [P, NG * CAP // P, MW], I32)
    val, bad = sb("slot_f", [EP, ET], F32), sb("slot_bad", [EP, ET], F32)
    over, pos = sb("slot_over", [EP, ET], F32), sb("slot_pos", [EP, ET], F32)
    slot = {s: sb(f"slot_{s}", [EP, ET], I32) for s in ends}
    pay = {(s, b): sb(f"pay_{s}{b}", [EP, UN, MW], I32) for s in ends for b in range(2)}
    idx = {(s, b): sb(f"idx_{s}{b}", [EP, UN], I32) for s in ends for b in range(2)}
    base = sb("round_base", [EP, ROUNDS], F32)
    lo = sb("round_lo", [EP, ROUNDS], F32)
    s_base, s_empty, s_fill, s_dve = sem("s_base"), sem("s_empty"), sem("s_fill"), sem("s_dve")
    s_filled = sem("s_filled")
    s_free = [sem(f"s_free{b}") for b in range(2)]
    s_order = sem("s_order")
    s_stage, s_clear = [sem(f"s_stage{b}") for b in range(2)], sem("s_clear")
    s_sent = {(s, b): sem(f"s_sent_{s}{b}") for s in ends for b in range(2)}
    HALF = ET // (2 * UN)
    REGION = NG * CAP
    OVER = float(1 << 23)
    assert ROUNDS * REGION < 1 << 23

    with nc.Block() as block:
        @block.sync
        def _(sp):
            r_count = sp.value_load(m.rounds[0:1, 0:1], min_val=1, max_val=ROUNDS)
            sp.wait_ge(s_empty, 1)
            with sp.Fori(0, r_count) as r:
                for s in ends:
                    sp.dma_start(m.meta[s][bass.ds(r * REGION, REGION), :].rearrange("(p a) w -> p (a w)", p=P),
                                 empty[:, :, :].rearrange("p a w -> p (a w)")).then_inc(s_fill, 16)
                sp.wait_ge(s_fill, r * 32 + 32)
                sp.sem_inc(s_filled, 1)
        @block.gpsimd
        def _(pool):
            r_count = pool.value_load(m.rounds[0:1, 0:1], min_val=1, max_val=ROUNDS)
            pool.memset(empty[:, :, 0:2], BIG).then_inc(s_clear, 1)
            pool.memset(empty[:, :, 2:3].bitcast(F32), -1.0).then_inc(s_clear, 1)
            pool.memset(empty[:, :, 3:MW], 0).then_inc(s_empty, 1)
            pool.iota(lo[:, :], [[CAP, ROUNDS]], base=0, channel_multiplier=0,
                      allow_small_or_imprecise_dtypes=True).then_inc(s_base, 1)
            with pool.Fori(0, r_count) as r:
                with pool.Fori(0, HALF) as i:
                    for b in range(2):
                        pool.wait_ge(s_filled, r + 1)
                        pool.wait_ge(s_stage[b], r * HALF + i + 1)
                        pool.sem_inc(s_order, 1)
                        for u in range(UN):
                            for s in ends:
                                pool.indirect_dma_start(
                                    m.meta[s][:, :], bass.IndirectOffsetOnAxis(ap=idx[s, b][:, u:u + 1], axis=0),
                                    pay[s, b][:, u, :], None, bounds_check=ROUNDS * REGION - 1,
                                    oob_is_err=False).then_inc(s_sent[s, b], 16)

        @block.scalar
        def _(act):
            r_count = act.value_load(m.rounds[0:1, 0:1], min_val=1, max_val=ROUNDS)
            for b in range(2):
                act.sem_inc(s_free[b], 1)
            with act.Fori(0, r_count) as r:
                with act.Fori(0, HALF) as i:
                    for b in range(2):
                        for s in ends:
                            act.wait_ge(s_sent[s, b], (r * HALF + i + 1) * (UN * 16))
                        act.sem_inc(s_free[b], 1)

        @block.vector
        def _(dve):
            r_count = dve.value_load(m.rounds[0:1, 0:1], min_val=1, max_val=ROUNDS)
            PER_ROUND = 16
            for b in range(2):
                for s in ends:
                    dve.memset(pay[s, b][:, :, :], 0)
            dve.wait_ge(s_clear, 2)
            dve.wait_ge(s_base, 1)
            dve.tensor_scalar(base[:, :], lo[:, :], float(NG), None, ALU.mult).then_inc(s_base, 1)
            dve.wait_ge(s_base, 2)
            with dve.Fori(0, r_count) as r:
                link = Link(dve, s_dve, r * PER_ROUND)
                for s in ends:
                    link(dve.tensor_scalar(val[:, :], rank[s][:, :], col(lo, r), None, ALU.subtract)).wait()
                    link(dve.tensor_scalar(bad[:, :], val[:, :], 0.0, OVER, ALU.is_lt, ALU.mult))
                    link(dve.tensor_scalar(over[:, :], val[:, :], float(CAP), OVER, ALU.is_ge, ALU.mult))
                    link(dve.tensor_scalar(pos[:, :], grp[s][:, :], float(CAP), col(base, r), ALU.mult, ALU.add)).wait()
                    link(dve.tensor_tensor(bad[:, :], bad[:, :], over[:, :], ALU.add))
                    link(dve.tensor_tensor(pos[:, :], pos[:, :], val[:, :], ALU.add)).wait()
                    link(dve.tensor_tensor(pos[:, :], pos[:, :], bad[:, :], ALU.add)).wait()
                    link(dve.tensor_copy(slot[s][:, :], pos[:, :]))
                    if s == "fwd":
                        link.wait()
                assert link.n == PER_ROUND
                with dve.Fori(0, HALF) as i:
                    for b in range(2):
                        dve.wait_ge(s_free[b], r * HALF + i + 1)
                        dve.wait_ge(s_dve, r * PER_ROUND + PER_ROUND)
                        c = (i * 2 + b) * UN
                        for s in ends:
                            p = pay[s, b]
                            dve.tensor_copy(p[:, :, W_NODE], col(other[s], c, UN))
                            dve.tensor_copy(p[:, :, W_COL].bitcast(F32), col(cols[s], c, UN))
                            dve.tensor_copy(p[:, :, W_PLAIN].bitcast(F32), col(ws[s], c, UN))
                            if s == "fwd":
                                dve.tensor_copy(p[:, :, W_TYPED], col(typed, c, UN))
                                dve.tensor_copy(p[:, :, W_EW].bitcast(F32), col(ew, c, UN))
                            last = dve.tensor_copy(idx[s, b][:, :], col(slot[s], c, UN))
                        last.then_inc(s_stage[b], 1)


def numbered(g):
    return g, g % 2, g // 2


def slots(eng, ahead, slot):
    ahead(*numbered(0))
    ahead(*numbered(1))
    slot(numbered(0), None)
    ahead(*numbered(2))
    slot(numbered(1), numbered(0))
    with eng.Fori(1, PAIRS - 1) as gp:
        ahead(gp * 2 + 1, 1, gp)
        slot((gp * 2, 0, gp), (gp * 2 - 1, 1, gp - 1))
        ahead(gp * 2 + 2, 0, gp + 1)
        slot((gp * 2 + 1, 1, gp), (gp * 2, 0, gp))
    ahead(*numbered(NG - 1))
    slot(numbered(NG - 2), numbered(NG - 3))
    slot(numbered(NG - 1), numbered(NG - 2))
    slot(None, numbered(NG - 1))


def no_edges(g, par, gi):
    pass


def pairs(eng, body):
    with eng.Fori(0, PAIRS) as gp:
        for par in range(2):
            body(gp * 2 + par, par, gp)


class Norm:

    def __init__(self, sc, m, scaled):
        sb, sem = sc.sb, sc.sem
        self.m, self.scaled = m, scaled
        self.st = [sb(f"n_st{p}", [P, J, 6], F32) for p in range(2)]
        self.mv = [sb(f"n_mv{p}", [P, J, 2], F32) for p in range(2)]
        self.sd, self.rs, self.nm = ([sb(f"{n}{p}", [P, J], F32) for p in range(2)] for n in ("n_sd", "n_rs", "n_nm"))
        self.s_order = sem("n_order")
        self.s_st, self.s_var, self.s_sd = sem("n_st"), sem("n_var"), sem("n_sd")
        self.s_rs, self.s_ln, self.s_h = sem("n_rs"), sem("n_ln"), sem("n_h")

    def stats(self, dve, x, g, par, gi):
        for j in range(J):
            last = dve.bn_stats(self.st[par][:, j, :], x[:, j, :])
        last.then_inc(self.s_st, 1)
        dve.wait_ge(self.s_st, g + 1)
        dve.sem_inc(self.s_order, 1)
        for j in range(J):
            last = dve.bn_aggr(self.mv[par][:, j, :], self.st[par][:, j, :])
        last.then_inc(self.s_var, 1)

    def affine(self, dve, g, par, gi):
        rs, mv = self.rs[par], self.mv[par]
        dve.wait_ge(self.s_sd, g + 1)
        dve.reciprocal(rs[:, :], self.sd[par][:, :]).then_inc(self.s_rs, 1)
        if self.scaled:
            dve.wait_ge(self.s_rs, g * 2 + 1)
            dve.sem_inc(self.s_order, 1)
            dve.tensor_tensor(rs[:, :], rs[:, :], col(self.m.dinv, g * J, J), ALU.mult).then_inc(self.s_rs, 1)
            dve.wait_ge(self.s_rs, g * 2 + 2)
        else:
            dve.wait_ge(self.s_rs, g + 1)
        dve.scalar_tensor_tensor(out=self.nm[par][:, :], in0=mv[:, :, 0], scalar=-1.0, in1=rs[:, :],
                                 op0=ALU.mult, op1=ALU.mult).then_inc(self.s_ln, 1)

    def roots(self, act, g, par, gi):
        act.wait_ge(self.s_var, g + 1)
        act.activation(self.sd[par][:, :], self.mv[par][:, :, 1], ACT.Sqrt, bias=self.m.eps[:, :]).then_inc(self.s_sd, 1)

    def relu(self, act, x, h, g, par, gi):
        act.wait_ge(self.s_ln, g + 1)
        for j in range(J):
            last = act.activation(h[:, j, :], x[:, j, :], ACT.Relu, bias=self.nm[par][:, j:j + 1],
                                  scale=self.rs[par][:, j:j + 1])
        last.then_inc(self.s_h, 1)


def v3(ap):
    return ap[:, :].rearrange("p (j d) -> p j d", j=J)


class Edges:

    def __init__(self, sc, m, stream, table, word, weight, agg):
        sb, sem = sc.sb, sc.sem
        self.m, self.meta, self.table, self.word, self.weight, self.agg = m, m.meta[stream], table, word, weight, agg
        self.slots = [sb(f"slots{p}", [P, TILES, MW], I32) for p in range(2)]
        self.hot = [[sb(f"onehot{p}_{k}", [P, GN], F32) for k in range(TILES)] for p in range(2)]
        self.s_slots = [sem(f"a_slots{p}") for p in range(2)]
        self.s_gath = [[sem(f"a_gath{p}_{k}") for k in range(TILES)] for p in range(2)]
        self.s_hot = [sem(f"a_hot{p}") for p in range(2)]
        self.s_summed = [sem(f"a_summed{p}") for p in range(2)]
        self.s_order = [sem("a_order_pool"), sem("a_order_dve")]

    def count(self, eng):
        return eng.value_load(self.m.rounds[0:1, 0:1], min_val=1, max_val=ROUNDS)

    def load(self, sp, par, n, g, r):
        sp.wait_ge(self.s_summed[par], n * TILES + 1)
        first = (r * NG + g) * CAP
        src = self.meta[first:first + CAP, :] if isinstance(first, int) else self.meta[bass.ds(first, CAP), :]
        sp.dma_start(self.slots[par][:, :, :].rearrange("p k w -> p (k w)"),
                     src.rearrange("(p k) w -> p (k w)", k=TILES)).then_inc(self.s_slots[par], 16)

    def load_more(self, sp, rc, g, par, gi):
        with sp.If(rc > 1):
            base = sp.snap(rc * gi)
            with sp.Fori(1, rc) as r:
                self.load(sp, par, base + r, g, r)

    def gather(self, pool, rc, g, par, gi):
        base = pool.snap(rc * gi)
        with pool.Fori(base, base + rc) as n:
            pool.wait_ge(self.s_slots[par], (n + 1) * 16)
            pool.wait_ge(self.s_summed[par], n * TILES + 1)
            pool.sem_inc(self.s_order[0], 1)
            for k in range(TILES):
                pool.indirect_dma_start(self.m.gath[par][k][:, 0:D], None, self.table,
                                        bass.IndirectOffsetOnAxis(ap=self.slots[par][:, k, self.word:self.word + 1], axis=0),
                                        bounds_check=self.table.shape[0] - 1,
                                        oob_is_err=False).then_inc(self.s_gath[par][k], 16)

    def onehots(self, dve, rc, g, par, gi):
        base = dve.snap(rc * gi)
        with dve.Fori(base, base + rc) as n:
            dve.wait_ge(self.s_slots[par], (n + 1) * 16)
            dve.wait_ge(self.s_summed[par], n * TILES + 1)
            for k in range(TILES):
                s = self.slots[par]
                node = s[:, k, W_COL:W_COL + 1].bitcast(F32)
                if self.weight is None:
                    ins = dve.tensor_scalar(self.hot[par][k][:, :], self.m.iota[:, :], node, None, ALU.is_equal)
                else:
                    w = s[:, k, self.weight:self.weight + 1].bitcast(F32)
                    ins = dve.tensor_scalar(self.hot[par][k][:, :], self.m.iota[:, :], node, w, ALU.is_equal, ALU.mult)
                ins.then_inc(self.s_hot[par], 1)

    def onehots_first(self, dve, rc):
        for g in range(2):
            self.onehots(dve, rc, *numbered(g))

    def onehots_next(self, dve, rc, g, par, gi):
        if not (isinstance(g, int) and g + 2 >= NG):
            self.onehots(dve, rc, g + 2, par, gi + 1)

    def sums(self, pe, rc, tile, g, par, gi):
        base = pe.snap(rc * gi)
        with pe.Fori(base, base + rc) as n:
            for k in range(TILES):
                pe.wait_ge(self.s_gath[par][k], (n + 1) * 16)
                pe.wait_ge(self.s_hot[par], n * TILES + k + 1)
                tile(self.m.gath[par][k], self.hot[par][k], self.agg[par]).then_inc(self.s_summed[par], 1)

    def wait_summed(self, eng, rc, g, par, gi):
        eng.wait_ge(self.s_summed[par], rc * (gi + 1) * TILES + 1)


def by_feature(pe):
    return lambda rows, hot, agg: pe.matmul(agg[:, :], rows[:, 0:D], hot[:, :], start=False, stop=True,
                                            skip_group_check=True)


SUMW = D + 1


def by_node(pe):
    def tile(rows, hot, agg):
        for j in range(J):
            last = pe.matmul(agg[:, j // 2, (j % 2) * SUMW:(j % 2 + 1) * SUMW], hot[:, j * P:(j + 1) * P],
                             rows[:, :], start=False, stop=True, skip_group_check=True)
        return last
    return tile


class Traffic:

    def __init__(self, sc, edges, edge_loads=(), node_loads=(), stores_a=(), ready_a=None, stores_b=(), ready_b=None,
                 ready_load=None, consts=(), lead=2, edge_lead=3):
        sem = sc.sem
        self.edges, self.edge_loads, self.node_loads, self.consts, self.lead = edges, edge_loads, node_loads, consts, lead
        self.stores = {"a": stores_a, "b": stores_b}
        self.ready, self.ready_load, self.edge_lead = {"a": ready_a, "b": ready_b}, ready_load, edge_lead
        self.s_own, self.s_in = [sem(f"t_own{p}") for p in range(2)], [sem(f"t_in{p}") for p in range(2)]
        self.s_out = {x: [sem(f"t_out_{x}{p}") for p in range(2)] for x in "ab"}
        self.s_stored = {x: sem(f"t_stored_{x}") for x in "ab"}
        self.s_const, self.s_order = sem("t_const"), sem("t_order")

    def wait_const(self, eng):
        eng.wait_ge(self.s_const, 16 * len(self.consts))

    def wait_own(self, eng, g, par, gi):
        eng.wait_ge(self.s_own[par], (gi + 1) * (16 * len(self.edge_loads)))

    def wait_in(self, eng, g, par, gi):
        eng.wait_ge(self.s_in[par], (gi + 1) * (16 * len(self.node_loads)))

    def wait_free(self, eng, x, g):
        eng.wait_ge(self.s_stored[x], g + 1)

    def program(self, sp):
        e = self.edges
        rc = e.count(sp) if e else None
        for x in "ab":
            sp.sem_inc(self.s_stored[x], 2)
        for to, frm in self.consts:
            sp.dma_start(to, frm).then_inc(self.s_const, 16)

        def edge_load(g, par, gi):
            if e:
                e.load(sp, par, rc * gi, g, 0)
            for buf, frm in self.edge_loads:
                sp.dma_start(buf[par][:, :], frm(g)).then_inc(self.s_own[par], 16)

        def node_load(g, par, gi):
            for buf, frm in self.node_loads:
                frm = frm(g)
                sp.dma_start(buf[par][0:frm.shape[0], :], frm).then_inc(self.s_in[par], 16)

        def wait(s, value):
            sp.wait_ge(s, value)
            sp.sem_inc(self.s_order, 1)

        def ready(x, group):
            if group and self.stores[x]:
                self.ready[x](wait, group[0])

        def store(x, group):
            if group and self.stores[x]:
                g, par, gi = group
                for buf, to in self.stores[x]:
                    to = to(g)
                    sp.dma_start(to, buf[par][0:to.shape[0], :]).then_inc(self.s_out[x][par], 16)

        def stored(x, group):
            if group is None or not self.stores[x]:
                return
            g, par, gi = group
            wait(self.s_out[x][par], (gi + 1) * (16 * len(self.stores[x])))
            sp.sem_inc(self.s_stored[x], 1)

        def edges_ahead(near, lead):
            if near[lead - 1] and e:
                e.load_more(sp, rc, *near[lead - 1])
            if near[lead]:
                edge_load(*near[lead])

        def step(near):
            if self.edge_lead == 3:
                edges_ahead(near, 3)
                ready("a", near[0])
                ready("b", near[-1])
                if near[self.lead]:
                    node_load(*near[self.lead])
            else:
                stored("b", near[-2])
                if near[-1]:
                    self.ready_load(wait, near[-1][0])
                if near[self.lead]:
                    node_load(*near[self.lead])
                edges_ahead(near, 4)
                ready("b", near[-1])
            store("a", near[0])
            store("b", near[-1])
            if self.edge_lead == 3:
                stored("a", near[-1])
                stored("b", near[-2])

        def static(s):
            step({d: numbered(s + d) if 0 <= s + d < NG else None for d in range(-2, 5)})

        edge_load(*numbered(0))
        edge_load(*numbered(1))
        for g in range(self.lead):
            node_load(*numbered(g))
        if e:
            for g in range(2):
                e.load_more(sp, rc, *numbered(g))
        edge_load(*numbered(2))
        if self.edge_lead == 4:
            e.load_more(sp, rc, *numbered(2))
            edge_load(*numbered(3))
        static(0)
        static(1)
        with sp.Fori(1, PAIRS - 2) as gp:
            for odd in range(2):
                step({d: (gp * 2 + odd + d, (odd + d) % 2, gp + (odd + d) // 2) for d in range(-2, 5)})
        for s in range(NG - 4, NG + 2):
            static(s)
        sp.wait_ge(self.s_const, 16 * len(self.consts)) if self.consts else None


def node_rows(ap, pad=True):
    return lambda g: rows(ap, g, P if pad or not isinstance(g, int) or g < NG - 1 else LAST_P)


def blocks(ap, n=P):
    return lambda g: group(ap, g, n)


def column(ap):
    return ap.rearrange("(p a) -> p a", a=1)


def line(ap):
    return ap.rearrange("(a n) -> a n", a=1)


def dense_in(nc, m, x):
    with nc.cleanup_on_exit():
        sc = Scope(nc, "dense")
        sb, sem = sc.sb, sc.sem
        norm = Norm(sc, m, scaled=True)
        xt = [sb(f"x{p}", [P, GN], F32) for p in range(2)]
        h = [sb(f"h{p}", [P, GN], F32) for p in range(2)]
        t = Traffic(sc, None, node_loads=[(xt, node_rows(x, pad=False))], stores_a=[(h, node_rows(m.A))],
                    ready_a=lambda wait, g: wait(norm.s_h, g + 1))
        with nc.Block() as block:
            @block.sync
            def _(sp):
                t.program(sp)

            @block.vector
            def _(dve):
                def slot(a, b):
                    if a:
                        t.wait_in(dve, *a)
                        norm.stats(dve, v3(xt[a[1]]), *a)
                        norm.affine(dve, *a)
                slots(dve, no_edges, slot)

            @block.scalar
            def _(act):
                def slot(a, b):
                    if a:
                        norm.roots(act, *a)
                        t.wait_free(act, "a", a[0])
                        norm.relu(act, v3(xt[a[1]]), v3(h[a[1]]), *a)
                slots(act, no_edges, slot)


class Typed:

    def __init__(self, sc, free):
        self.pt = [sc.ps(f"pt{i}", [P, TYPES * D], F32) for i in range(2)]
        self.tab = [sc.sb(f"tab{p}", [P, J * TYPES * D], F32) for p in range(2)]
        self.W = sc.sb("Wtyped", [P, TYPES * D], F32)
        self.s_pt, self.s_tab = sc.sem("y_pt"), [sc.sem(f"y_tab{i}") for i in range(2)]
        self.free = free

    def consts(self, W):
        return [(self.W[:, r * D:(r + 1) * D], W[r]) for r in range(TYPES)]

    def start(self, pe):
        for s in self.s_tab:
            pe.sem_inc(s, 1)

    def products(self, pe, hT, g, par, gi):
        for j in range(J):
            pe.wait_ge(self.s_tab[j % 2], g * 2 + j // 2 + 1)
            pe.matmul(self.pt[j % 2][:, :], hT[:, j * P:(j + 1) * P], self.W[:, :], start=True,
                      stop=True).then_inc(self.s_pt, 1)

    def copies(self, eng, copy, i, g, par, gi):
        self.free(eng, g)
        for j in range(i, J, 2):
            eng.wait_ge(self.s_pt, g * J + j + 1)
            copy(self.tab[par][:, j * TYPES * D:(j + 1) * TYPES * D], self.pt[i][:, :]).then_inc(self.s_tab[i], 1)

    def ready(self, wait, g):
        for s in self.s_tab:
            wait(s, g * 2 + 3)


def weights_and_bias(pe, pn, aggS, W, sq, b):
    for j in range(J):
        pe.matmul(pn[:, j, :], aggS[:, j * P:(j + 1) * P], W[:, :], start=True, stop=False)
        last = pe.matmul(pn[:, j, :], sq[:, j * P:(j + 1) * P], b[:, :], start=False, stop=True)
    return last


def own_rows(pe, agg, own, ident):
    for j in range(J):
        pe.matmul(agg[:, j * P:(j + 1) * P], own[:, j * D:(j + 1) * D], ident[:, :], start=(j == 0), stop=True,
                  skip_group_check=True)


def credits(eng, *sems):
    for s in sems:
        eng.sem_inc(s, 1)


def gcn_first(nc, m, x, W, b, Wtyped):
    with nc.cleanup_on_exit():
        sc = Scope(nc, "gcn_first")
        sb, ps, sem = sc.sb, sc.ps, sc.sem
        agg = [ps(f"agg{p}", [P, GN], F32) for p in range(2)]
        pn, pT = ps("pn", [P, J, D], F32), ps("pT", [P, GN], F32)
        e = Edges(sc, m, "fwd", m.A, W_NODE, None, agg)
        norm = Norm(sc, m, scaled=False)
        own, xt, xo, aggS, h, hT = ([sb(f"{n}{p}", [P, GN], F32) for p in range(2)] for n in ("own", "xt", "xo", "aggS", "h", "hT"))
        sq = [sb(f"sq{p}", [1, GN], F32) for p in range(2)]
        Wt, bt = sb("Wt", [P, D], F32), sb("bt", [1, D], F32)
        s_ev, s_pn, s_x1, s_pT, s_hT = (sem(n) for n in ("ev", "pn", "x1", "pT", "hT"))
        y = Typed(sc, lambda eng, g: t.wait_free(eng, "b", g))

        def ready_b(wait, g):
            wait(s_hT, g + 2)
            y.ready(wait, g)
        t = Traffic(sc, e, edge_loads=[(own, node_rows(m.A))],
                    node_loads=[(xt, node_rows(x, pad=False)), (sq, blocks(m.sq, 1))],
                    stores_a=[(xo, node_rows(m.X))], ready_a=lambda wait, g: wait(norm.s_h, g + 1),
                    stores_b=[(hT, blocks(m.hT[0])), (y.tab, node_rows(m.typed[0]))], ready_b=ready_b,
                    consts=[(Wt[:, :], W), (bt[:, :], line(b))] + y.consts(Wtyped))

        with nc.Block() as block:
            @block.sync
            def _(sp):
                t.program(sp)

            @block.gpsimd
            def _(pool):
                rc = e.count(pool)
                pairs(pool, lambda *g: e.gather(pool, rc, *g))

            @block.tensor
            def _(pe):
                rc = e.count(pe)
                t.wait_const(pe)

                def ahead(g, par, gi):
                    pe.wait_ge(s_ev, g + 1)
                    t.wait_own(pe, g, par, gi)
                    own_rows(pe, agg[par], own[par], m.ident)
                    e.sums(pe, rc, by_feature(pe), g, par, gi)

                def slot(a, b):
                    if a:
                        g, par, gi = a
                        pe.wait_ge(s_ev, g + 3)
                        pe.wait_ge(s_x1, g + 1)
                        t.wait_in(pe, *a)
                        weights_and_bias(pe, pn, aggS[par], Wt, sq[par], bt).then_inc(s_pn, 1)
                    if b:
                        g, par, gi = b
                        pe.wait_ge(norm.s_h, g + 1)
                        pe.wait_ge(s_hT, g + 1)
                        for j in range(J):
                            last = pe.transpose(pT[:, j * P:(j + 1) * P], h[par][:, j * D:(j + 1) * D], m.ident[:, :])
                        last.then_inc(s_pT, 1)
                        pe.wait_ge(s_hT, g + 2)
                        y.products(pe, hT[par], *b)
                credits(pe, s_ev, s_ev, s_x1, s_hT, *e.s_summed)
                y.start(pe)
                slots(pe, ahead, slot)

            @block.vector
            def _(dve):
                rc = e.count(dve)

                def slot(a, b):
                    if a:
                        g, par, gi = a
                        dve.wait_ge(s_pn, g + 1)
                        t.wait_in(dve, *a)
                        t.wait_free(dve, "a", g)
                        dve.sem_inc(norm.s_order, 1)
                        for j in range(J):
                            last = dve.scalar_tensor_tensor(out=v3(xo[par])[:, j, :], in0=pn[:, j, :],
                                                            scalar=col(m.dinv, g * J + j), in1=v3(xt[par])[:, j, :],
                                                            op0=ALU.mult, op1=ALU.add)
                        last.then_inc(s_x1, 1)
                        dve.wait_ge(s_x1, g + 2)
                        norm.stats(dve, v3(xo[par]), *a)
                    if b:
                        y.copies(dve, dve.tensor_copy, 1, *b)
                    if a:
                        e.onehots_next(dve, rc, *a)
                        norm.affine(dve, *a)
                e.onehots_first(dve, rc)
                slots(dve, no_edges, slot)

            @block.scalar
            def _(act):
                rc = e.count(act)

                def slot(a, b):
                    if a:
                        e.wait_summed(act, rc, *a)
                        act.copy(aggS[a[1]][:, :], agg[a[1]][:, :]).then_inc(s_ev, 1)
                    if b:
                        t.wait_free(act, "b", b[0])
                        act.wait_ge(s_pT, b[0] + 1)
                        act.copy(hT[b[1]][:, :], pT[:, :]).then_inc(s_hT, 1)
                        y.copies(act, act.copy, 0, *b)
                    if a:
                        norm.roots(act, *a)
                        norm.relu(act, v3(xo[a[1]]), v3(h[a[1]]), *a)
                slots(act, no_edges, slot)


def rgcn_first(nc, m, root, b, Wtyped):
    with nc.cleanup_on_exit():
        sc = Scope(nc, "rgcn_first")
        sb, ps, sem = sc.sb, sc.ps, sc.sem
        agg = [ps(f"agg{p}", [P, GN], F32) for p in range(2)]
        e = Edges(sc, m, "fwd", typed_rows(m.typed[0]), W_TYPED, W_EW, agg)
        own, hT = ([sb(f"{n}{p}", [P, GN], F32) for p in range(2)] for n in ("own", "hT"))
        Rt, bt = sb("Rt", [P, D], F32), sb("bt", [P, 1], F32)
        s_ev = sem("ev")
        y = Typed(sc, lambda eng, g: t.wait_free(eng, "a", g))

        def ready_a(wait, g):
            wait(s_ev, g + 3)
            y.ready(wait, g)
        t = Traffic(sc, e, edge_loads=[(own, blocks(m.hT[0]))],
                    stores_a=[(hT, blocks(m.hT[1])), (y.tab, node_rows(m.typed[1]))], ready_a=ready_a,
                    consts=[(Rt[:, :], root), (bt[:, :], column(b))] + y.consts(Wtyped))

        with nc.Block() as block:
            @block.sync
            def _(sp):
                t.program(sp)

            @block.gpsimd
            def _(pool):
                rc = e.count(pool)
                pairs(pool, lambda *g: e.gather(pool, rc, *g))

            @block.tensor
            def _(pe):
                rc = e.count(pe)
                t.wait_const(pe)

                def ahead(g, par, gi):
                    pe.wait_ge(s_ev, g + 1)
                    t.wait_own(pe, g, par, gi)
                    pe.matmul(agg[par][:, :], Rt[:, :], own[par][:, :], start=True, stop=True, skip_group_check=True)
                    e.sums(pe, rc, by_feature(pe), g, par, gi)

                def slot(a, b):
                    if a:
                        pe.wait_ge(s_ev, a[0] + 3)
                        y.products(pe, hT[a[1]], *a)
                credits(pe, s_ev, s_ev, *e.s_summed)
                y.start(pe)
                slots(pe, ahead, slot)

            @block.vector
            def _(dve):
                rc = e.count(dve)

                def slot(a, b):
                    if a:
                        y.copies(dve, dve.tensor_copy, 1, *a)
                        e.onehots_next(dve, rc, *a)
                e.onehots_first(dve, rc)
                slots(dve, no_edges, slot)

            @block.scalar
            def _(act):
                rc = e.count(act)
                t.wait_const(act)

                def slot(a, b):
                    if a:
                        e.wait_summed(act, rc, *a)
                        t.wait_free(act, "a", a[0])
                        act.activation(hT[a[1]][:, :], agg[a[1]][:, :], ACT.Relu, bias=bt[:, :]).then_inc(s_ev, 1)
                        y.copies(act, act.copy, 0, *a)
                slots(act, no_edges, slot)


def typed_rows(ap):
    return ap.rearrange("n (r d) -> (n r) d", r=TYPES)


def rgcn_second(nc, m, root, b):
    with nc.cleanup_on_exit():
        sc = Scope(nc, "rgcn_second")
        sb, ps, sem = sc.sb, sc.ps, sc.sem
        agg = [ps(f"agg{p}", [P, GN], F32) for p in range(2)]
        pn, pT = ps("pn", [P, J, D], F32), ps("pT", [P, GN], F32)
        e = Edges(sc, m, "fwd", typed_rows(m.typed[1]), W_TYPED, W_EW, agg)
        norm = Norm(sc, m, scaled=False)
        own, xt, xo, aggS, h = ([sb(f"{n}{p}", [P, GN], F32) for p in range(2)] for n in ("own", "xt", "xo", "aggS", "h"))
        Rt, bt = sb("Rt", [P, D], F32), sb("bt", [P, 1], F32)
        stats = sb("stats", [P, NG * 6], F32)
        s_ev, s_pn, s_x2, s_pT, s_bn, s_mv = (sem(n) for n in ("ev", "pn", "x2", "pT", "bn", "mv"))
        t = Traffic(sc, e, edge_loads=[(own, blocks(m.hT[1]))], node_loads=[(xt, node_rows(m.X))],
                    stores_a=[(xo, node_rows(m.X)), (h, node_rows(m.B))], ready_a=lambda wait, g: wait(norm.s_h, g + 1),
                    consts=[(Rt[:, :], root), (bt[:, :], column(b))])

        with nc.Block() as block:
            @block.sync
            def _(sp):
                t.program(sp)

            @block.gpsimd
            def _(pool):
                rc = e.count(pool)
                pairs(pool, lambda *g: e.gather(pool, rc, *g))

            @block.tensor
            def _(pe):
                rc = e.count(pe)
                t.wait_const(pe)

                def ahead(g, par, gi):
                    pe.wait_ge(s_ev, g + 1)
                    t.wait_own(pe, g, par, gi)
                    pe.matmul(agg[par][:, :], Rt[:, :], own[par][:, :], start=True, stop=True, skip_group_check=True)
                    e.sums(pe, rc, by_feature(pe), g, par, gi)

                def slot(a, b):
                    if a:
                        g, par, gi = a
                        pe.wait_ge(s_ev, g + 3)
                        pe.wait_ge(s_x2, g + 1)
                        for j in range(J):
                            last = pe.transpose(pn[:, j, :], aggS[par][:, j * P:(j + 1) * P], m.ident[:, :])
                        last.then_inc(s_pn, 1)
                    if b:
                        g, par, gi = b
                        pe.wait_ge(norm.s_h, g + 1)
                        pe.wait_ge(s_bn, g + 1)
                        for j in range(J):
                            last = pe.transpose(pT[:, j * P:(j + 1) * P], h[par][:, j * D:(j + 1) * D], m.ident[:, :])
                        last.then_inc(s_pT, 1)
                credits(pe, s_ev, s_ev, s_x2, s_bn, s_pT, s_pT, *e.s_summed)
                slots(pe, ahead, slot)

            @block.vector
            def _(dve):
                rc = e.count(dve)

                def slot(a, b):
                    if a:
                        g, par, gi = a
                        e.onehots_next(dve, rc, *a)
                        dve.wait_ge(s_pn, g + 1)
                        t.wait_in(dve, *a)
                        t.wait_free(dve, "a", g)
                        dve.tensor_tensor(v3(xo[par]), v3(xt[par]), pn[:, :, :], ALU.add).then_inc(s_x2, 1)
                        dve.wait_ge(s_x2, g + 2)
                        norm.stats(dve, v3(xo[par]), *a)
                    if b:
                        g = b[0]
                        dve.wait_ge(s_pT, g + 3)
                        dve.sem_inc(norm.s_order, 1)
                        f = pT[:, :].rearrange("p (j n) -> p j n", j=J)
                        if isinstance(g, int) and g == NG - 1:
                            f = f[:, :, 0:LAST_P]
                        dve.bn_stats(col(stats, g * 6, 6), f).then_inc(s_bn, 1)
                    if a:
                        norm.affine(dve, *a)
                e.onehots_first(dve, rc)
                slots(dve, no_edges, slot)
                dve.wait_ge(s_bn, NG + 1)
                dve.bn_aggr(m.bn[:, :], stats[:, :]).then_inc(s_mv, 1)
                dve.wait_ge(s_mv, 1)

            @block.scalar
            def _(act):
                rc = e.count(act)
                t.wait_const(act)

                def slot(a, b):
                    if a:
                        g, par, gi = a
                        e.wait_summed(act, rc, *a)
                        act.activation(aggS[par][:, :], agg[par][:, :], ACT.Identity, bias=bt[:, :]).then_inc(s_ev, 1)
                        norm.roots(act, *a)
                        t.wait_free(act, "a", g)
                        act.wait_ge(s_pT, g + 1)
                        norm.relu(act, v3(xo[par]), v3(h[par]), *a)
                slots(act, no_edges, slot)


def weight_sums(nc, m):
    with nc.cleanup_on_exit():
        sc = Scope(nc, "weight_sums")
        sb, ps, sem = sc.sb, sc.ps, sc.sem
        agg = [ps(f"agg{p}", [P, 2, GN], F32) for p in range(2)]
        pT = ps("pT", [P, GN], F32)
        e = Edges(sc, m, "rev", m.B, W_NODE, W_PLAIN, agg)
        sums = [sb(f"sums{p}", [P, J, SUMW], F32) for p in range(2)]
        aT = [sb(f"aT{p}", [P, GN], F32) for p in range(2)]
        zeros = sb("zeros", [1, GN], BF16)
        s_ev, s_pT, s_aT, s_zero, s_order = (sem(n) for n in ("ev", "pT", "aT", "zero", "order"))
        t = Traffic(sc, e, stores_a=[(aT, blocks(m.aggT))], ready_a=lambda wait, g: wait(s_aT, g * 2 + 5))

        with nc.Block() as block:
            @block.sync
            def _(sp):
                t.program(sp)

            @block.gpsimd
            def _(pool):
                rc = e.count(pool)
                pairs(pool, lambda *g: e.gather(pool, rc, *g))

            @block.tensor
            def _(pe):
                rc = e.count(pe)
                pe.wait_ge(s_zero, 1)

                def ahead(g, par, gi):
                    pe.wait_ge(s_ev, g + 1)
                    zero_banks(pe, agg[par], zeros)
                    e.sums(pe, rc, by_node(pe), g, par, gi)

                def slot(a, b):
                    if a:
                        g, par, gi = a
                        pe.wait_ge(s_ev, g + 3)
                        pe.wait_ge(s_aT, g * 2 + 3)
                        for j in range(J):
                            last = pe.transpose(pT[:, j * P:(j + 1) * P], sums[par][:, j, 0:D], m.ident[:, :])
                        last.then_inc(s_pT, 1)
                credits(pe, s_ev, s_ev, s_aT, s_aT, s_aT, *e.s_summed)
                slots(pe, ahead, slot)

            @block.vector
            def _(dve):
                rc = e.count(dve)
                dve.memset(zeros[:, :], 0.0).then_inc(s_zero, 1)

                def slot(a, b):
                    if a:
                        g, par, gi = a
                        e.onehots_next(dve, rc, *a)
                        dve.wait_ge(s_ev, g + 3)
                        dve.sem_inc(s_order, 1)
                        dve.tensor_copy(col(m.sum_out, g * J, J), sums[par][:, :, D]).then_inc(s_aT, 1)
                        dve.wait_ge(s_pT, g + 1)
                        t.wait_free(dve, "a", g)
                        dve.tensor_copy(aT[par][:, :], pT[:, :]).then_inc(s_aT, 1)
                e.onehots_first(dve, rc)
                slots(dve, no_edges, slot)

            @block.scalar
            def _(act):
                rc = e.count(act)

                def slot(a, b):
                    if a:
                        e.wait_summed(act, rc, *a)
                        act.wait_ge(s_aT, a[0] * 2 + 1)
                        copy_sums(act, sums[a[1]], agg[a[1]]).then_inc(s_ev, 1)
                slots(act, no_edges, slot)


def zero_banks(pe, agg, zeros):
    for i in range(2):
        pe.matmul(agg[:, i, :], zeros[:, 0:P], zeros[:, :], start=True, stop=True, skip_group_check=True)


def copy_sums(act, sums, agg):
    for i in range(2):
        last = act.copy(sums[:, 2 * i:2 * i + 2, :].rearrange("p j d -> p (j d)"), agg[:, i, 0:2 * SUMW])
    return last


class Gates:

    def __init__(self, sc, m, p):
        self.sc, self.m, self.p = sc, m, p
        sb = sc.sb
        self.M = {k: sb(f"M_{k}", [P, 2 * D], F32) for k in ("in", "out", "own")}
        self.v = {k: sb(f"v_{k}", [P, 2 * D], F32) for k in ("in", "out")}
        self.const = sb("const", [P, J * 2 * D], F32)
        self.srow, self.trow = sb("srow", [P, J * D], F32), sb("trow", [P, J * D], F32)

    def build(self, nc):
        sc, m, p = self.sc, self.m, self.p
        sb, sem = sc.sb, sc.sem
        W = {k: sb(f"W_{k}", [P, D], F32) for k in ("in", "out")}
        WT = {k: sb(f"WT_{k}", [P, D], F32) for k in ("in", "out")}
        G = {k: sb(f"G_{k}", [P, 2 * D], F32) for k in ("in", "out", "own")}
        C = {k: sb(f"C_{k}", [P, 2 * D], F32) for k in ("in", "out")}
        cols = {k: sb(f"c_{k}", [P, 1], F32) for k in ("b_in", "b_out", "gamma", "beta", "sd", "rs", "s", "t", "mt")}
        wide = {k: sb(f"wide_{k}", [P, P], F32) for k in ("s", "t", "b_in", "b_out")}
        ones, bg = sb("ones", [P, P], F32), sb("bg", [1, 2 * D], F32)
        pc = {k: sc.ps(f"pc_{k}", [P, GN], F32) for k in ("in", "out", "own", "rows")}
        s_ld, s_d, s_a, s_p = sem("f_load"), sem("f_dve"), sem("f_act"), sem("f_pe")
        with nc.Block() as block:
            @block.sync
            def _(sp):
                loads = [(W["in"], p["W_in"]), (W["out"], p["W_out"]), (G["in"], p["Wg_in"][0:D, :]),
                         (G["out"], p["Wg_in"][D:2 * D, :]), (G["own"], p["Wg_out"]), (bg, line(p["bg_in"])),
                         (cols["b_in"], column(p["b_in"])), (cols["b_out"], column(p["b_out"])),
                         (cols["gamma"], column(p["bn_gamma"])), (cols["beta"], column(p["bn_beta"]))]
                for to, frm in loads:
                    sp.dma_start(to[:, :], frm).then_inc(s_ld, 16)
                sp.wait_ge(s_ld, 16 * 10)

            @block.scalar
            def _(act):
                act.activation(cols["sd"][:, :], m.bn[:, 1:2], ACT.Sqrt, bias=m.eps[:, :]).then_inc(s_a, 1)

            @block.vector
            def _(dve):
                link = Link(dve, s_d)
                link(dve.memset(ones[:, :], 1.0))
                dve.wait_ge(s_ld, 16 * 10)
                dve.wait_ge(s_a, 1)
                link(dve.reciprocal(cols["rs"][:, :], cols["sd"][:, :])).wait()
                link(dve.tensor_tensor(cols["s"][:, :], cols["rs"][:, :], cols["gamma"][:, :], ALU.mult)).wait()
                link(dve.tensor_tensor(cols["mt"][:, :], m.bn[:, 0:1], cols["s"][:, :], ALU.mult)).wait()
                link(dve.tensor_tensor(cols["t"][:, :], cols["beta"][:, :], cols["mt"][:, :], ALU.subtract)).wait()
                for k in wide:
                    link(dve.tensor_scalar(wide[k][:, :], ones[:, :], cols[k][:, :], None, ALU.mult))
                dve.wait_ge(s_p, 1)
                for k in W:
                    link(dve.tensor_copy(WT[k][:, :], pc[k][:, 0:D]))
                link.wait()
                dve.wait_ge(s_p, 2)
                for k in W:
                    link(dve.tensor_copy(C[k][:, :], pc[k][:, 0:2 * D]))
                    link(dve.tensor_scalar(self.M[k][:, :], pc[k][:, 0:2 * D], cols["s"][:, :], None, ALU.mult))
                link(dve.tensor_scalar(self.M["own"][:, :], G["own"][:, :], cols["s"][:, :], None, ALU.mult))
                dve.wait_ge(s_p, 3)
                for k in W:
                    link(dve.tensor_copy(self.v[k][:, :], pc[k][:, 0:2 * D]))
                for j in range(J):
                    link(dve.tensor_copy(self.const[:, j * 2 * D:(j + 1) * 2 * D], pc["own"][:, 0:2 * D]))
                    link(dve.tensor_copy(self.srow[:, j * D:(j + 1) * D], pc["rows"][:, 0:D]))
                    link(dve.tensor_copy(self.trow[:, j * D:(j + 1) * D], pc["rows"][:, D:2 * D]))
                link.wait()

            @block.tensor
            def _(pe):
                pe.wait_ge(s_ld, 16 * 10)
                for k in W:
                    last = pe.transpose(pc[k][:, 0:D], W[k][:, :], m.ident[:, :])
                last.then_inc(s_p, 1)
                pe.wait_ge(s_d, 11)
                for k in W:
                    last = pe.matmul(pc[k][:, 0:2 * D], WT[k][:, :], G[k][:, :], start=True, stop=True)
                last.then_inc(s_p, 1)
                pe.wait_ge(s_d, 15)
                for k in W:
                    pe.matmul(pc[k][:, 0:2 * D], wide["t"][:, :], C[k][:, :], start=True, stop=False)
                    pe.matmul(pc[k][:, 0:2 * D], wide["b_" + k][:, :], G[k][:, :], start=False, stop=True)
                pe.matmul(pc["own"][:, 0:2 * D], wide["t"][:, :], G["own"][:, :], start=True, stop=False)
                pe.matmul(pc["own"][:, 0:2 * D], ones[0:1, :], bg[:, :], start=False, stop=True)
                pe.matmul(pc["rows"][:, 0:D], wide["s"][:, :], m.ident[:, :], start=True, stop=True)
                pe.matmul(pc["rows"][:, D:2 * D], wide["t"][:, :], m.ident[:, :], start=True, stop=True).then_inc(s_p, 1)


def gated(nc, m, p):
    with nc.cleanup_on_exit():
        sc = Scope(nc, "gated")
        sb, sem = sc.sb, sc.sem
        w = Gates(sc, m, p)
        with nc.cleanup_on_exit():
            w.build(nc)
        agg = [sc.ps(f"agg{q}", [P, 2, GN], F32) for q in range(2)]
        pT, pF, pG = sc.ps("pT", [P, GN], F32), sc.ps("pF", [P, GN], F32), sc.ps("pG", [P, J * 2 * D], F32)
        e = Edges(sc, m, "fwd", m.B, W_NODE, W_PLAIN, agg)
        norm = Norm(sc, m, scaled=True)
        sums = [sb(f"sums{q}", [P, J, SUMW], F32) for q in range(2)]
        f, xt, xo, oT, aT, fT, h, xb, d = ([sb(f"{n}{q}", [P, GN], F32) for q in range(2)]
                                       for n in ("f", "xt", "xo", "oT", "aT", "fT", "h", "xb", "d"))
        u = [sb(f"u{q}", [P, J, 2 * D], F32) for q in range(2)]
        zeros = sb("zeros", [1, GN], BF16)
        s_ev, s_pT, s_T, s_pG, s_u, s_gate, s_x, s_zero, s_order = (
            sem(n) for n in ("ev", "pT", "T", "pG", "u", "gate", "x", "zero", "order"))
        OWN = 6
        t = Traffic(sc, e, node_loads=[(oT, blocks(m.aggT)), (f, node_rows(m.B)), (xt, node_rows(m.X))],
                    stores_b=[(xo, node_rows(m.X)), (h, node_rows(m.A))], ready_b=lambda wait, g: wait(norm.s_h, g + 1),
                    ready_load=lambda wait, g: wait(s_x, (g + 1) * OWN), lead=1, edge_lead=4)

        with nc.Block() as block:
            @block.sync
            def _(sp):
                t.program(sp)

            @block.gpsimd
            def _(pool):
                rc = e.count(pool)
                pairs(pool, lambda *g: e.gather(pool, rc, *g))

            @block.tensor
            def _(pe):
                rc = e.count(pe)
                pe.wait_ge(s_zero, 1)

                def ahead(g, par, gi):
                    pe.wait_ge(s_ev, g + 1)
                    zero_banks(pe, agg[par], zeros)
                    e.sums(pe, rc, by_node(pe), g, par, gi)

                def slot(a, b):
                    if b:
                        g, par, gi = b
                        pe.wait_ge(s_T, g * 2 + 3)
                        pe.wait_ge(s_u, g * 3 + 1)
                        for j in range(J):
                            c = slice(j * P, (j + 1) * P)
                            out = pG[:, j * 2 * D:(j + 1) * 2 * D]
                            pe.matmul(out, aT[par][:, c], w.M["in"][:, :], start=True, stop=False)
                            pe.matmul(out, oT[par][:, c], w.M["out"][:, :], start=False, stop=False)
                            last = pe.matmul(out, fT[par][:, c], w.M["own"][:, :], start=False, stop=True)
                        last.then_inc(s_pG, 1)
                    if a:
                        g, par, gi = a
                        pe.wait_ge(s_ev, g + 3)
                        t.wait_in(pe, *a)
                        pe.wait_ge(s_T, g * 2 + 1)
                        for j in range(J):
                            pe.transpose(pT[:, j * P:(j + 1) * P], sums[par][:, j, 0:D], m.ident[:, :])
                            last = pe.transpose(pF[:, j * P:(j + 1) * P], f[par][:, j * D:(j + 1) * D], m.ident[:, :])
                        last.then_inc(s_pT, 1)
                credits(pe, s_ev, s_ev, s_T, s_u, *e.s_summed)
                slots(pe, ahead, slot)

            @block.vector
            def _(dve):
                rc = e.count(dve)
                dve.memset(zeros[:, :], 0.0).then_inc(s_zero, 1)
                def slot(a, b):
                    if not b:
                        e.onehots_next(dve, rc, *a)
                        return
                    g, par, gi = b

                    def linked(ins):
                        ins.then_inc(s_x, 1)
                        n[0] += 1

                    def wait_own():
                        dve.wait_ge(s_x, g * OWN + n[0])
                    n = [0]
                    t.wait_in(dve, *b)
                    linked(dve.tensor_tensor(xb[par][:, :], f[par][:, :], w.srow[:, :], ALU.mult))
                    wait_own()
                    linked(dve.tensor_tensor(xb[par][:, :], xb[par][:, :], w.trow[:, :], ALU.add))
                    if a:
                        e.onehots_next(dve, rc, *a)
                    dve.wait_ge(s_pG, g + 1)
                    dve.tensor_tensor(u[par][:, :, :].rearrange("p j d -> p (j d)"), pG[:, :], w.const[:, :],
                                      ALU.add).then_inc(s_u, 1)
                    for i, (k, scalar) in enumerate((("in", lambda j: sums[par][:, j, D:SUMW]),
                                                     ("out", lambda j: col(m.sum_out, g * J + j)))):
                        dve.wait_ge(s_u, g * 3 + 2 + i)
                        dve.sem_inc(s_order, 1)
                        for j in range(J):
                            last = dve.scalar_tensor_tensor(out=u[par][:, j, :], in0=w.v[k][:, :], scalar=scalar(j),
                                                            in1=u[par][:, j, :], op0=ALU.mult, op1=ALU.add)
                        last.then_inc(s_u, 1)
                    dve.wait_ge(s_gate, g + 1)
                    wait_own()
                    gate, new = u[par][:, :, 0:D], u[par][:, :, D:2 * D]
                    linked(dve.tensor_tensor(v3(d[par]), v3(xb[par]), new, ALU.subtract))
                    t.wait_free(dve, "b", g)
                    linked(dve.tensor_tensor(v3(xo[par]), v3(xt[par]), new, ALU.add))
                    wait_own()
                    linked(dve.tensor_tensor(v3(d[par]), v3(d[par]), gate, ALU.mult))
                    wait_own()
                    linked(dve.tensor_tensor(xo[par][:, :], xo[par][:, :], d[par][:, :], ALU.add))
                    wait_own()
                    assert n[0] == OWN
                    norm.stats(dve, v3(xo[par]), *b)
                    norm.affine(dve, *b)
                e.onehots_first(dve, rc)
                slots(dve, no_edges, slot)

            @block.scalar
            def _(act):
                rc = e.count(act)

                def slot(a, b):
                    if a:
                        g, par, gi = a
                        e.wait_summed(act, rc, *a)
                        copy_sums(act, sums[par], agg[par]).then_inc(s_ev, 1)
                        act.wait_ge(s_pT, g + 1)
                        act.copy(aT[par][:, :], pT[:, :]).then_inc(s_T, 1)
                        act.copy(fT[par][:, :], pF[:, :]).then_inc(s_T, 1)
                    if b:
                        g, par, gi = b
                        act.wait_ge(s_u, g * 3 + 4)
                        act.activation(u[par][:, :, 0:D], u[par][:, :, 0:D], ACT.Sigmoid)
                        act.activation(u[par][:, :, D:2 * D], u[par][:, :, D:2 * D], ACT.Tanh).then_inc(s_gate, 1)
                        norm.roots(act, *b)
                        t.wait_free(act, "b", g)
                        norm.relu(act, v3(xo[par]), v3(h[par]), *b)
                slots(act, no_edges, slot)


def gcn_middle(nc, m, name, source, target, W, b):
    with nc.cleanup_on_exit():
        sc = Scope(nc, name)
        sb, ps, sem = sc.sb, sc.ps, sc.sem
        agg = [ps(f"agg{p}", [P, GN], F32) for p in range(2)]
        pn = ps("pn", [P, J, D], F32)
        e = Edges(sc, m, "fwd", source, W_NODE, None, agg)
        own, aggS, h = ([sb(f"{n}{p}", [P, GN], F32) for p in range(2)] for n in ("own", "aggS", "h"))
        sq = [sb(f"sq{p}", [1, GN], F32) for p in range(2)]
        Wt, bt = sb("Wt", [P, D], F32), sb("bt", [1, D], F32)
        s_ev, s_pn, s_h, s_order = (sem(n) for n in ("ev", "pn", "h", "order"))
        t = Traffic(sc, e, edge_loads=[(own, node_rows(source))], node_loads=[(sq, blocks(m.sq, 1))],
                    stores_a=[(h, node_rows(target))], ready_a=lambda wait, g: wait(s_h, g + 2),
                    consts=[(Wt[:, :], W), (bt[:, :], line(b))])

        with nc.Block() as block:
            @block.sync
            def _(sp):
                t.program(sp)

            @block.gpsimd
            def _(pool):
                rc = e.count(pool)
                pairs(pool, lambda *g: e.gather(pool, rc, *g))

            @block.tensor
            def _(pe):
                rc = e.count(pe)
                t.wait_const(pe)
                gcn_products(pe, m, e, t, rc, agg, own, aggS, pn, Wt, sq, bt, s_ev, s_pn, s_h)

            @block.vector
            def _(dve):
                rc = e.count(dve)
                pairs(dve, lambda *g: e.onehots(dve, rc, *g))

            @block.scalar
            def _(act):
                rc = e.count(act)

                def slot(a, b):
                    if a:
                        g, par, gi = a
                        e.wait_summed(act, rc, *a)
                        act.copy(aggS[par][:, :], agg[par][:, :]).then_inc(s_ev, 1)
                        t.wait_free(act, "a", g)
                        act.wait_ge(s_pn, g + 1)
                        act.sem_inc(s_order, 1)
                        for j in range(J):
                            last = act.activation(h[par][:, j * D:(j + 1) * D], pn[:, j, :], ACT.Relu,
                                                  scale=col(m.dinv2, g * J + j))
                        last.then_inc(s_h, 1)
                slots(act, no_edges, slot)


def gcn_products(pe, m, e, t, rc, agg, own, aggS, pn, Wt, sq, bt, s_ev, s_pn, s_used):
    def ahead(g, par, gi):
        pe.wait_ge(s_ev, g + 1)
        t.wait_own(pe, g, par, gi)
        own_rows(pe, agg[par], own[par], m.ident)
        e.sums(pe, rc, by_feature(pe), g, par, gi)

    def slot(a, b):
        if a:
            g, par, gi = a
            pe.wait_ge(s_ev, g + 3)
            pe.wait_ge(s_used, g + 1)
            t.wait_in(pe, *a)
            weights_and_bias(pe, pn, aggS[par], Wt, sq[par], bt).then_inc(s_pn, 1)
    credits(pe, s_ev, s_ev, s_used, *e.s_summed)
    slots(pe, ahead, slot)


def gcn_last(nc, m, source, W, b, out):
    with nc.cleanup_on_exit():
        sc = Scope(nc, "gcn_last")
        sb, ps, sem = sc.sb, sc.ps, sc.sem
        agg = [ps(f"agg{p}", [P, GN], F32) for p in range(2)]
        pn = ps("pn", [P, J, D], F32)
        e = Edges(sc, m, "fwd", source, W_NODE, None, agg)
        own, aggS, xt, xo = ([sb(f"{n}{p}", [P, GN], F32) for p in range(2)] for n in ("own", "aggS", "xt", "xo"))
        sq = [sb(f"sq{p}", [1, GN], F32) for p in range(2)]
        Wt, bt = sb("Wt", [P, D], F32), sb("bt", [1, D], F32)
        s_ev, s_pn, s_x, s_order = (sem(n) for n in ("ev", "pn", "x", "order"))
        t = Traffic(sc, e, edge_loads=[(own, node_rows(source))], node_loads=[(xt, node_rows(m.X)), (sq, blocks(m.sq, 1))],
                    stores_a=[(xo, node_rows(out, pad=False))], ready_a=lambda wait, g: wait(s_x, g + 2),
                    consts=[(Wt[:, :], W), (bt[:, :], line(b))])

        with nc.Block() as block:
            @block.sync
            def _(sp):
                t.program(sp)

            @block.gpsimd
            def _(pool):
                rc = e.count(pool)
                pairs(pool, lambda *g: e.gather(pool, rc, *g))

            @block.tensor
            def _(pe):
                rc = e.count(pe)
                t.wait_const(pe)
                gcn_products(pe, m, e, t, rc, agg, own, aggS, pn, Wt, sq, bt, s_ev, s_pn, s_x)

            @block.vector
            def _(dve):
                rc = e.count(dve)

                def slot(a, b):
                    if a:
                        g, par, gi = a
                        e.onehots_next(dve, rc, *a)
                        dve.wait_ge(s_pn, g + 1)
                        t.wait_in(dve, *a)
                        t.wait_free(dve, "a", g)
                        dve.sem_inc(s_order, 1)
                        for j in range(J):
                            last = dve.scalar_tensor_tensor(out=v3(xo[par])[:, j, :], in0=pn[:, j, :],
                                                            scalar=col(m.dinv, g * J + j), in1=v3(xt[par])[:, j, :],
                                                            op0=ALU.mult, op1=ALU.add)
                        last.then_inc(s_x, 1)
                e.onehots_first(dve, rc)
                slots(dve, no_edges, slot)

            @block.scalar
            def _(act):
                rc = e.count(act)

                def slot(a, b):
                    if a:
                        e.wait_summed(act, rc, *a)
                        act.copy(aggS[a[1]][:, :], agg[a[1]][:, :]).then_inc(s_ev, 1)
                slots(act, no_edges, slot)


def program(nc, p, out):
    m = Mem(nc)
    constants(nc, m)
    place_edges(nc, m, p["src"], p["dst"], p["edge_type_4"], p["edge_weight"], p["edge_weight_n2"])
    dense_in(nc, m, p["x"])
    gcn_first(nc, m, p["x"], p["L0_gnn_W"], p["L0_gnn_b"], p["L1_gnn_W1"])
    rgcn_first(nc, m, p["L1_gnn_root1"], p["L1_gnn_b1"], p["L1_gnn_W2"])
    rgcn_second(nc, m, p["L1_gnn_root2"], p["L1_gnn_b2"])
    weight_sums(nc, m)
    gated(nc, m, {n[len("L2_gnn_"):]: a for n, a in p.items() if n.startswith("L2_gnn_")})
    gcn_middle(nc, m, "gcn_2", m.A, m.B, p["L3_gnn_W0"], p["L3_gnn_b0"])
    gcn_middle(nc, m, "gcn_3", m.B, m.A, p["L3_gnn_W1"], p["L3_gnn_b1"])
    gcn_last(nc, m, m.A, p["L3_gnn_W2"], p["L3_gnn_b2"], out)


def kernel(**inputs):
    import numpy as _np
    import concourse.bacc as _bacc
    from concourse import mybir as _mybir
    from concourse.bass_utils import run_bass_kernel_spmd as _run

    nc = _bacc.Bacc("TRN2", target_bir_lowering=False, num_devices=1)
    arrays, args = {}, {}
    for name, value in inputs.items():
        a = _np.ascontiguousarray(value)
        arrays[f"in_{name}"] = a
        args[name] = nc.dram_tensor(f"in_{name}", a.shape, _mybir.dt.from_np(a.dtype), kind="ExternalInput").ap()
    out = nc.dram_tensor("out_0", (NODES, D), F32, kind="ExternalOutput").ap()
    program(nc, args, out)
    r = _run(nc, [arrays], core_ids=[0])
    return r.results[0]["out_0"]
```
